# Optimizing a Trainium2 kernel written in Bass

```python
import numpy as np
import jax
import jax.numpy as jnp

def _softmax(x, axis=-1):
    return jax.nn.softmax(x, axis=axis)

def _gelu(x):
    return jax.nn.gelu(x, approximate=True)

def _silu(x):
    return jax.nn.silu(x)

def _sigmoid(x):
    return jax.nn.sigmoid(x)

def _layernorm(x, axis=-1, eps=1e-05):
    m = jnp.mean(x, axis=axis, keepdims=True)
    v = jnp.var(x, axis=axis, keepdims=True)
    return (x - m) / jnp.sqrt(v + eps)

def _scatter_add(tgt, idx, src, axis=0):
    return tgt.at[idx].add(src)

def _segment_sum(src, seg, n):
    return jax.ops.segment_sum(src, seg, n)
kernel_name = 'mk_gnn_preln_d4_gnn_r8_65e676'

def setup_inputs(seed: int=0):
    np.random.seed(seed)
    _w = jnp.asarray

    def _rec_inputs():
        import jax
        import jax.numpy as jnp
        _gk = jax.random.key(seed)
        x = -0.0001006 + 1 * jax.random.normal(jax.random.fold_in(_gk, 1), (12500, 48), jnp.float32)
        _s = jax.random.randint(jax.random.fold_in(_gk, 2), (200000,), 0, 12500, jnp.int32)
        _d = jax.random.randint(jax.random.fold_in(_gk, 3), (200000,), 0, 12500, jnp.int32)
        _loop = jnp.arange(12500, dtype=jnp.int32)
        src = jnp.concatenate([_s, _d, _loop])
        dst = jnp.concatenate([_d, _s, _loop])
        _o = jnp.argsort(dst, stable=True)
        src = src[_o]
        dst = dst[_o]
        edge_attr_48 = -4.21973e-05 + 0.999841 * jax.random.normal(jax.random.fold_in(_gk, 12), (412500, 48), jnp.float32)
        edge_weight = jax.random.uniform(jax.random.fold_in(_gk, 14), (412500,), jnp.float32, 0.0, 0.999998)
        return (x, src, dst, edge_attr_48, edge_weight)
    x, src, dst, edge_attr_48, edge_weight = _rec_inputs()

    def _L0_gnn_setup():
        import jax, jax.numpy as jnp
        import numpy as np
        N_NODES = 12500
        N_EDGES = 200000
        D_IN = 48
        D_OUT = 48
        key = jax.random.key(seed)
        k1, k2, k3, k4, k5 = jax.random.split(key, 5)
        x = jax.random.normal(k1, (N_NODES, D_IN), dtype=jnp.float32)
        init_range = np.sqrt(6.0 / (D_IN + D_OUT)).astype(np.float32)
        w = jax.random.uniform(k2, (D_IN, D_OUT), dtype=jnp.float32, minval=-init_range, maxval=init_range)
        b = jnp.zeros((D_OUT,), dtype=jnp.float32)
        edge_src = jax.random.randint(k3, (N_EDGES,), 0, N_NODES, dtype=jnp.int32)
        edge_dst = jax.random.randint(k4, (N_EDGES,), 0, N_NODES, dtype=jnp.int32)
        adj_vals = jax.random.uniform(k5, (N_EDGES,), dtype=jnp.float32)
        return {'x': x, 'w': w, 'b': b, 'edge_src': edge_src, 'edge_dst': edge_dst, 'adj_vals': adj_vals}
    _L0_gnn_all = _L0_gnn_setup()
    _L0_gnn_in = {k: v for k, v in _L0_gnn_all.items() if k in ('w', 'b')}
    del _L0_gnn_all

    def _L1_gnn_setup():
        import jax, jax.numpy as jnp
        import numpy as np
        NUM_NODES = 12500
        key = jax.random.key(seed)
        k1, k2, k3 = jax.random.split(key, 3)
        x = jax.random.normal(k1, (NUM_NODES, 48), dtype=jnp.float32)
        edge_index = jax.random.randint(k2, (2, 200000), 0, NUM_NODES, dtype=jnp.int64)
        edge_weight = jax.random.uniform(k3, (200000,), dtype=jnp.float32)
        return {'x': x, 'edge_index': edge_index, 'edge_weight': edge_weight}
    _L1_gnn_all = _L1_gnn_setup()
    _L1_gnn_in = {k: v for k, v in _L1_gnn_all.items() if k in ()}
    del _L1_gnn_all

    def _L2_gnn_setup():
        import jax, jax.numpy as jnp
        import numpy as np
        N_NODES = 12500
        N_EDGES = 200000
        D_FEAT = 48
        K = 2

        def _spmm(edge_weight, edge_src, edge_dst, x):
            msgs = edge_weight[:, None] * x[edge_src]
            return jax.ops.segment_sum(msgs, edge_dst, num_segments=N_NODES)
        key = jax.random.key(seed)
        k1, k2, k3, k4 = jax.random.split(key, 4)
        x = jax.random.normal(k1, (N_NODES, D_FEAT), dtype=jnp.float32)
        edge_weight = jax.random.uniform(k2, (N_EDGES,), dtype=jnp.float32)
        edge_src = jax.random.randint(k3, (N_EDGES,), 0, N_NODES, dtype=jnp.int32)
        edge_dst = jax.random.randint(k4, (N_EDGES,), 0, N_NODES, dtype=jnp.int32)
        return {'x': x, 'edge_weight': edge_weight, 'edge_src': edge_src, 'edge_dst': edge_dst}
    _L2_gnn_all = _L2_gnn_setup()
    _L2_gnn_in = {k: v for k, v in _L2_gnn_all.items() if k in ()}
    del _L2_gnn_all

    def _L3_gnn_setup():
        import jax, jax.numpy as jnp
        import numpy as np
        N_NODES = 12500
        N_EDGES = 200000
        D_FEAT = 48
        key = jax.random.key(seed)
        k1, k2, k3, k4 = jax.random.split(key, 4)
        node_feat = jax.random.normal(k1, (N_NODES, D_FEAT), dtype=jnp.float32)
        edge_feat = jax.random.normal(k2, (N_EDGES, D_FEAT), dtype=jnp.float32)
        src = jax.random.randint(k3, (N_EDGES,), 0, N_NODES, dtype=jnp.int32)
        dst = jax.random.randint(k4, (N_EDGES,), 0, N_NODES, dtype=jnp.int32)
        eps = jnp.zeros((1,), dtype=jnp.float32)
        return {'node_feat': node_feat, 'edge_feat': edge_feat, 'src': src, 'dst': dst, 'eps': eps}
    _L3_gnn_all = _L3_gnn_setup()
    _L3_gnn_in = {k: v for k, v in _L3_gnn_all.items() if k in ('eps',)}
    del _L3_gnn_all
    return {'x': x, 'src': src, 'dst': dst, 'edge_attr_48': edge_attr_48, 'edge_weight': edge_weight, 'L0_gnn_w': _L0_gnn_in['w'], 'L0_gnn_b': _L0_gnn_in['b'], 'L3_gnn_eps': _L3_gnn_in['eps']}

def reference(x, src, dst, edge_attr_48, edge_weight, L0_gnn_w, L0_gnn_b, L3_gnn_eps):
    import jax
    import jax.numpy as jnp

    def _L0_gnn_ref(x, w, b, edge_src, edge_dst, adj_vals):
        import jax, jax.numpy as jnp
        import numpy as np
        N_NODES = 12500
        N_EDGES = 200000
        D_IN = 48
        D_OUT = 48
        xw = jnp.matmul(x, w)
        msgs = adj_vals[:, None] * xw[edge_src]
        agg = jax.ops.segment_sum(msgs, edge_dst, num_segments=N_NODES)
        return jax.nn.relu(agg + b)

    def _L1_gnn_ref(x, edge_index, edge_weight):
        import jax, jax.numpy as jnp
        import numpy as np
        NUM_NODES = 12500
        src, dst = (edge_index[0], edge_index[1])
        msgs = x[src] * edge_weight[:, None]
        out = jax.ops.segment_sum(msgs, dst, num_segments=NUM_NODES)
        return out

    def _L2_gnn_ref(x, edge_weight, edge_src, edge_dst):
        import jax, jax.numpy as jnp
        import numpy as np
        N_NODES = 12500
        N_EDGES = 200000
        D_FEAT = 48
        K = 2

        def _spmm(edge_weight, edge_src, edge_dst, x):
            msgs = edge_weight[:, None] * x[edge_src]
            return jax.ops.segment_sum(msgs, edge_dst, num_segments=N_NODES)
        for _ in range(K):
            x = _spmm(edge_weight, edge_src, edge_dst, x)
        return x

    def _L3_gnn_ref(node_feat, edge_feat, src, dst, eps):
        import jax, jax.numpy as jnp
        import numpy as np
        N_NODES = 12500
        N_EDGES = 200000
        D_FEAT = 48
        m = jax.nn.relu(node_feat[src] + edge_feat)
        neigh = jax.ops.segment_sum(m, dst, num_segments=N_NODES)
        return (1.0 + eps[0]) * node_feat + neigh
    edge_index = jnp.stack([src, dst])
    h = jnp.maximum(_layernorm(x, axis=-1), 0.0)
    x = x + _L0_gnn_ref(h, L0_gnn_w, L0_gnn_b, src, dst, edge_weight)
    h = jnp.maximum(_layernorm(x, axis=-1), 0.0)
    x = x + _L1_gnn_ref(h, edge_index, edge_weight)
    h = jnp.maximum(_layernorm(x, axis=-1), 0.0)
    x = x + _L2_gnn_ref(h, edge_weight, src, dst)
    h = jnp.maximum(_layernorm(x, axis=-1), 0.0)
    x = x + _L3_gnn_ref(h, edge_attr_48, src, dst, L3_gnn_eps)
    return x

_drawn_inputs = setup_inputs


def setup_inputs(seed=0):
    import zlib

    import numpy as np

    out = dict(_drawn_inputs(seed))
    spreads = {'L0_gnn_b': (0.0, 0.355)}
    factors = {'edge_attr_48': 4.413}
    for name, (base, spread) in spreads.items():
        noise = np.random.default_rng([zlib.crc32(name.encode()), seed]).standard_normal(out[name].shape)
        drawn = base * np.exp(spread * noise) if base else spread * noise
        out[name] = jnp.asarray(drawn.astype(out[name].dtype))
    for name, factor in factors.items():
        out[name] = (out[name] * factor).astype(out[name].dtype)
    return out
```

```python
import concourse.bass as bass
from concourse import mybir
from contextlib import ExitStack


def gnn_kernel(nc, x, src, dst, edge_attr, edge_weight, weight, bias, eps, out):
    fp32, int32 = mybir.dt.float32, mybir.dt.int32
    ALU, ACT, AX = mybir.AluOpType, mybir.ActivationFunctionType, mybir.AxisListType

    N, D = x.shape
    E = src.shape[0]
    P = 128
    CHUNKS = 8
    SUPER = CHUNKS * P
    WINDOW_BITS = 7
    WINDOW = 1 << WINDOW_BITS
    RING = 4
    ROUNDS = -(-E // (SUPER * RING))
    S = ROUNDS * RING
    FULL, REST = divmod(E, SUPER)
    REST_P, REST_J = divmod(REST, CHUNKS)
    GROUPS = -(-S // P)
    HALF = CHUNKS // 2
    T = -(-N // P)
    NP = P * T
    LAST_P, LAST_T = divmod(N, T)
    LAST_P16 = LAST_P // 16 * 16
    ACC = NP + WINDOW
    PER_BANK = 512 // D
    LN_EPS = 1e-5
    NEVER = -1.0e38

    h_dram = nc.dram_tensor("h_rows", [NP, D], fp32).ap()
    h_tiles = h_dram.rearrange("(p t) d -> p t d", t=T)

    ctx = ExitStack()
    with ctx:
        def sb(name, shape, dt=fp32):
            return ctx.enter_context(nc.sbuf_tensor(name, shape, dt))

        edges = sb("edges", [P, S, 3, CHUNKS])
        base_row = sb("base_row", [1, S], int32)
        span_row = sb("span_row", [1, S])
        span_max = sb("span_max", [1, 1], int32)
        iota = sb("iota", [P, WINDOW])
        ident = sb("ident", [P, P])
        w_sb = sb("w_sb", [D, D])
        bias_sb = sb("bias_sb", [P, D])
        eps_sb = sb("eps_sb", [P, 1])
        x_sb = sb("x_sb", [P, T, D])
        h_sb = sb("h_sb", [P, T, D])
        scratch = sb("scratch", [P, T, D])
        acc = sb("acc", [D, ACC])
        iota_now = sb("iota_now", [P, WINDOW])
        base_now = sb("base_now", [1, S], int32)

        def sem(name):
            return ctx.enter_context(nc.semaphore(name))

        banks = [ctx.enter_context(nc.psum_tensor(f"bank{i}", [P, 512], fp32)) for i in range(8)]

        def group_rows(g):
            n = min(P, S - g * P)
            return n, max(0, min(n, FULL - g * P))

        def prepare():
            with ExitStack() as prep:
                raw = prep.enter_context(nc.sbuf_tensor("raw", [P, 2, SUPER], int32))
                flat = prep.enter_context(nc.sbuf_tensor("flat", [P, 3, SUPER], fp32))
                ends = prep.enter_context(nc.sbuf_tensor("ends", [P, 2], fp32))
                iota_int = prep.enter_context(nc.sbuf_tensor("iota_int", [P, WINDOW], int32))
                turned = [banks[i][:, 0:HALF * P].rearrange("p (j s) -> p j s", j=HALF) for i in range(2)]
                turned_ends = banks[2][:, 0:2 * P].rearrange("p (i s) -> p i s", i=2)
                const_ready, pool_step = sem("const_ready"), sem("pool_step")
                raw_loaded, pads_set = sem("raw_loaded"), sem("pads_set")
                flat_ready, dve_step = sem("flat_ready"), sem("dve_step")
                turned_ready, turned_used = sem("turned_ready"), [sem("turned_used0"), sem("turned_used1")]
                ends_turned, ends_used = sem("ends_turned"), sem("ends_used")
                x_pad_set, x_loaded, small_loaded = sem("x_pad_set"), sem("x_loaded"), sem("small_loaded")

                with nc.Block() as block:
                    @block.gpsimd
                    def _(pool):
                        pool.memset(x_sb[:, :, :], 0.0).then_inc(x_pad_set, 1)
                        pool.iota(iota_int[:, :], pattern=[[1, WINDOW]], base=0,
                                  channel_multiplier=0).then_inc(pool_step, 1)
                        pool.memset(ident[:, :], 0.0).then_inc(pool_step, 1)
                        pool.wait_ge(pool_step, 2)
                        pool.tensor_copy(iota[:, :], iota_int[:, :]).then_inc(const_ready, 1)
                        pool.affine_select(out=ident[:, :], in_=ident[:, :], compare_op=ALU.not_equal,
                                           fill=1.0, base=0, pattern=[[-1, P]], channel_multiplier=1)\
                            .then_inc(const_ready, 1)
                        pool.memset(acc[:, :], 0.0).then_inc(const_ready, 1)

                    @block.sync
                    def _(sp):
                        for g in range(GROUPS):
                            n, full = group_rows(g)
                            if full < n:
                                sp.wait_ge(pads_set, 3)
                            elif g > 0:
                                sp.wait_ge(flat_ready, 2 * g)
                                sp.wait_ge(turned_ready, 6 * g)
                            e0 = g * P * SUPER
                            for a, rows_in in ((src, raw[:, 0, :]), (dst, raw[:, 1, :]),
                                               (edge_weight, flat[:, 1, :])):
                                if full:
                                    sp.dma_start(rows_in[0:full, :], a[e0:e0 + full * SUPER]
                                                 .rearrange("(s e) -> s e", e=SUPER)).then_inc(raw_loaded, 16)
                                if full < n and REST:
                                    sp.dma_start(rows_in[full:full + 1, 0:REST], a[FULL * SUPER:E]
                                                 .rearrange("(s e) -> s e", s=1)).then_inc(raw_loaded, 16)

                    @block.scalar
                    def _(act):
                        act.dma_start(w_sb[:, :], weight).then_inc(small_loaded, 16)
                        act.dma_start(bias_sb[:, :], bias.rearrange("(a d) -> a d", a=1)
                                      .to_broadcast([P, D])).then_inc(small_loaded, 16)
                        act.dma_start(eps_sb[:, :], eps.rearrange("(a d) -> a d", a=1)
                                      .to_broadcast([P, 1])).then_inc(small_loaded, 16)
                        act.wait_ge(x_pad_set, 1)
                        for p0, p1 in ((0, LAST_P16), (LAST_P16, LAST_P)):
                            act.dma_start(x_sb[p0:p1, :, :], x[p0 * T:p1 * T, :]
                                          .rearrange("(p t) d -> p t d", t=T)).then_inc(x_loaded, 16)
                        act.dma_start(x_sb[LAST_P:LAST_P + 1, 0:LAST_T, :], x[LAST_P * T:N, :]
                                      .rearrange("(p t) d -> p t d", p=1)).then_inc(x_loaded, 16)
                        for g in range(GROUPS):
                            n, _full = group_rows(g)
                            for a in range(3):
                                act.wait_ge(turned_ready, 6 * g + 2 * a + 2)
                                act.activation(edges[:, g * P:g * P + n, a, HALF:CHUNKS],
                                               turned[1][:, :, 0:n].rearrange("p j s -> p s j"),
                                               ACT.Copy).then_inc(turned_used[1], 1)
                        act.wait_ge(small_loaded, 48)
                        act.wait_ge(x_loaded, 48)

                    @block.tensor
                    def _(pe):
                        pe.wait_ge(const_ready, 3)
                        for g in range(GROUPS):
                            n, _full = group_rows(g)
                            pe.wait_ge(flat_ready, 2 * (g + 1))
                            if g > 0:
                                pe.wait_ge(ends_used, g)
                            for i in range(2):
                                last = pe.transpose(turned_ends[0:1, i, 0:n], ends[0:n, i:i + 1], ident[0:n, 0:n])
                            last.then_inc(ends_turned, 1)
                            for a in range(3):
                                row = flat[0:n, a, :].rearrange("s (p j) -> s j p", j=CHUNKS)
                                for half in range(2):
                                    if 3 * g + a > 0:
                                        pe.wait_ge(turned_used[half], 3 * g + a)
                                    for j in range(HALF):
                                        last = pe.transpose(turned[half][:, j, 0:n],
                                                            row[:, HALF * half + j, :], ident[0:n, 0:n])
                                    last.then_inc(turned_ready, 1)

                    @block.vector
                    def _(dve):
                        steps = [0]

                        def step(instruction):
                            steps[0] += 1
                            instruction.then_inc(dve_step, 1)
                            dve.wait_ge(dve_step, steps[0])

                        loads = 0
                        for g in range(GROUPS):
                            n, full = group_rows(g)
                            if g > 0:
                                dve.wait_ge(turned_ready, 6 * g)
                            if full < n:
                                dve.memset(raw[:, 0, :], 0).then_inc(pads_set, 1)
                                dve.memset(raw[:, 1, :], N - 1).then_inc(pads_set, 1)
                                dve.memset(flat[:, 1, :], 0.0).then_inc(pads_set, 1)
                            loads += 3 * ((full > 0) + (full < n and REST > 0))
                            dve.wait_ge(raw_loaded, 16 * loads)
                            dve.tensor_copy(flat[0:n, 2, :], raw[0:n, 0, :]).then_inc(flat_ready, 1)
                            step(dve.tensor_copy(flat[0:n, 0, :], raw[0:n, 1, :]))
                            step(dve.tensor_reduce(ends[0:n, 0:1], flat[0:n, 0, :], AX.X, ALU.min))
                            step(dve.tensor_scalar(flat[0:n, 0, :], flat[0:n, 0, :], ends[0:n, 0:1], None,
                                                   ALU.subtract))
                            dve.tensor_reduce(ends[0:n, 1:2], flat[0:n, 0, :], AX.X, ALU.max)\
                                .then_inc(flat_ready, 1)
                            dve.wait_ge(ends_turned, g + 1)
                            step(dve.tensor_copy(base_row[0:1, g * P:g * P + n], turned_ends[0:1, 0, 0:n]))
                            step(dve.tensor_copy(span_row[0:1, g * P:g * P + n], turned_ends[0:1, 1, 0:n]))
                            dve.sem_inc(ends_used, 1)
                            for a in range(3):
                                dve.wait_ge(turned_ready, 6 * g + 2 * a + 1)
                                dve.tensor_copy(edges[:, g * P:g * P + n, a, 0:HALF],
                                                turned[0][:, :, 0:n].rearrange("p j s -> p s j"))\
                                    .then_inc(turned_used[0], 1)
                        step(dve.tensor_reduce(span_max[0:1, 0:1], span_row[0:1, :], AX.X, ALU.max))

        stats = sb("stats", [P, 3, T])
        acc_turned, acc_used, up_step = sem("acc_turned"), sem("acc_used"), sem("up_step")
        centred, squared = sem("centred"), sem("squared")
        var_ready, std_ready = sem("var_ready"), sem("std_ready")
        rows_ready, rows_stored = sem("rows_ready"), sem("rows_stored")
        in_update = [acc_turned, acc_used, up_step, centred, squared, var_ready, std_ready, rows_ready,
                     rows_stored]

        def update(kind, first=False):
            PARTS = 2
            cuts = [T * i // PARTS for i in range(PARTS + 1)]
            tiles = [(t, min(t + PER_BANK, cuts[i + 1])) for i in range(PARTS)
                     for t in range(cuts[i], cuts[i + 1], PER_BANK)]
            norm = kind != "hop" and kind != "last"
            with nc.Block() as block:
                if not first:
                    @block.tensor
                    def _(pe):
                        right = w_sb[:, :] if kind == "project" else ident[0:D, 0:D]
                        for i, (t0, t1) in enumerate(tiles):
                            if i >= 4:
                                pe.wait_ge(acc_used, i - 3)
                            for t in range(t0, t1):
                                last = pe.matmul(banks[4 + i % 4][:, (t - t0) * D:(t - t0 + 1) * D],
                                                 acc[:, t:t + (P - 1) * T + 1:T], right,
                                                 start=True, stop=True)
                            last.then_inc(acc_turned, 1)


                if kind != "last":
                    @block.gpsimd
                    def _(pool):
                        pool.tensor_copy(iota_now[:, :], iota[:, :])
                        pool.tensor_copy(base_now[:, :], base_row[:, :])
                        if not first:
                            pool.wait_ge(acc_turned, len(tiles))
                            pool.memset(acc[:, :], 0.0)

                @block.vector
                def _(dve):
                    steps = [0]

                    def step(instruction):
                        steps[0] += 1
                        instruction.then_inc(up_step, 1)
                        dve.wait_ge(up_step, steps[0])

                    if kind == "last":
                        step(dve.tensor_scalar(eps_sb[:, :], eps_sb[:, :], 1.0, None, ALU.add))
                        step(dve.scalar_tensor_tensor(x_sb[:, :, :], h_sb[:, :, :], eps_sb[:, 0:1],
                                                      x_sb[:, :, :], ALU.mult, ALU.add))
                    i = 0
                    for part in range(PARTS):
                        c0, c1 = cuts[part], cuts[part + 1]
                        while not first and i < len(tiles) and tiles[i][0] < c1:
                            t0, t1 = tiles[i]
                            new = banks[4 + i % 4][:, 0:(t1 - t0) * D].rearrange("p (t d) -> p t d", d=D)
                            xs = x_sb[:, t0:t1, :]
                            dve.wait_ge(acc_turned, i + 1)
                            if kind == "project":
                                step(dve.tensor_tensor(scratch[:, t0:t1, :], new, bias_sb[:, :].unsqueeze(1)
                                                       .to_broadcast([P, t1 - t0, D]), ALU.add))
                                dve.sem_inc(acc_used, 1)
                                step(dve.scalar_tensor_tensor(xs, scratch[:, t0:t1, :], 0.0, xs,
                                                              ALU.max, ALU.add))
                            elif kind == "hop":
                                step(dve.tensor_copy(scratch[:, t0:t1, :], new))
                                dve.sem_inc(acc_used, 1)
                            else:
                                step(dve.tensor_tensor(xs, new, xs, ALU.add))
                                dve.sem_inc(acc_used, 1)
                            i += 1
                        if norm:
                            xs, hs = x_sb[:, c0:c1, :], h_sb[:, c0:c1, :]
                            total, mean, var = (stats[:, k, c0:c1] for k in range(3))
                            wide = [P, c1 - c0, D]
                            step(dve.tensor_reduce(total, xs, AX.X, ALU.add))
                            step(dve.tensor_scalar(mean, total, 1.0 / D, None, ALU.mult))
                            dve.tensor_tensor(hs, xs, mean.unsqueeze(2).to_broadcast(wide), ALU.subtract)\
                                .then_inc(centred, 1)
                        else:
                            dve.sem_inc(rows_ready, 1)
                    if norm:
                        for part in range(PARTS):
                            c0, c1 = cuts[part], cuts[part + 1]
                            _total, _mean, var = (stats[:, k, c0:c1] for k in range(3))
                            dve.wait_ge(squared, part + 1)
                            step(dve.tensor_reduce(var, scratch[:, c0:c1, :], AX.X, ALU.add))
                            dve.tensor_scalar(var, var, 1.0 / D, LN_EPS, ALU.mult, ALU.add).then_inc(var_ready, 1)
                        for part in range(PARTS):
                            c0, c1 = cuts[part], cuts[part + 1]
                            hs = h_sb[:, c0:c1, :]
                            std, inverse, _var = (stats[:, k, c0:c1] for k in range(3))
                            dve.wait_ge(std_ready, part + 1)
                            step(dve.reciprocal(inverse, std))
                            dve.scalar_tensor_tensor(hs, hs, 0.0, inverse.unsqueeze(2)
                                                     .to_broadcast([P, c1 - c0, D]),
                                                     ALU.max, ALU.mult).then_inc(rows_ready, 1)

                if norm:
                    @block.scalar
                    def _(act):
                        for part in range(PARTS):
                            c0, c1 = cuts[part], cuts[part + 1]
                            act.wait_ge(centred, part + 1)
                            act.activation(scratch[:, c0:c1, :], h_sb[:, c0:c1, :], ACT.Square)\
                                .then_inc(squared, 1)
                        for part in range(PARTS):
                            c0, c1 = cuts[part], cuts[part + 1]
                            act.wait_ge(var_ready, part + 1)
                            act.activation(stats[:, 0, c0:c1], stats[:, 2, c0:c1], ACT.Sqrt)\
                                .then_inc(std_ready, 1)

                @block.sync
                def _(sp):
                    for part in range(PARTS):
                        c0, c1 = cuts[part], cuts[part + 1]
                        sp.wait_ge(rows_ready, part + 1)
                        if kind != "last":
                            rows_now = scratch if kind == "hop" else h_sb
                            sp.dma_start(h_tiles[:, c0:c1, :], rows_now[:, c0:c1, :]).then_inc(rows_stored, 16)
                        else:
                            for p0, p1 in ((0, LAST_P16), (LAST_P16, LAST_P)):
                                sp.dma_start(out[p0 * T:p1 * T, :].rearrange("(p t) d -> p t d", t=T)
                                             [:, c0:c1, :], x_sb[p0:p1, c0:c1, :]).then_inc(rows_stored, 16)
                            c1 = min(c1, LAST_T)
                            sp.dma_start(out[LAST_P * T:N, :].rearrange("(p t) d -> p t d", p=1)
                                         [:, c0:c1, :], x_sb[LAST_P:LAST_P + 1, c0:c1, :]).then_inc(rows_stored, 16)
                    sp.wait_ge(rows_stored, 16 * PARTS * (3 if kind == "last" else 1))

            with nc.Block() as block:
                @block.gpsimd
                def _(pool):
                    for signal in in_update:
                        pool.sem_clear(signal)

        src_idx = sb("src_idx", [P, RING, CHUNKS], int32)
        dst_w = sb("dst_w", [P, RING, 2, CHUNKS])
        rows = sb("rows", [P, RING, CHUNKS, D])
        select = sb("select", [P, RING, CHUNKS, WINDOW])
        features = sb("features", [P, RING, CHUNKS, D])
        idx_staged, dst_staged = sem("idx_staged"), sem("dst_staged")
        gathered = [sem(f"gathered{r}") for r in range(RING)]
        selected, multiplied, added = sem("selected"), sem("multiplied"), sem("added")
        features_loaded = [sem(f"features_loaded{r}") for r in range(RING)]
        summed, messages_ready = sem("summed"), sem("messages_ready")
        pad_set, begun = sem("pad_set"), sem("begun")
        part_loaded = sem("part_loaded")
        in_round = [idx_staged, dst_staged, *gathered, selected, multiplied, added,
                    *features_loaded, summed, messages_ready, pad_set, begun, part_loaded]

        def edge_sum(with_features=False):
            with nc.Fori(0, (widest >> WINDOW_BITS) + 1):
                with nc.Block() as block:
                    @block.gpsimd
                    def _(pool):
                        with pool.Fori(0, ROUNDS) as i:
                            for r in range(RING):
                                pool.wait_ge(idx_staged, i * RING + (r + 1))
                                pool.wait_ge(multiplied, i * RING + (r + 1))
                                pool.sem_inc(begun, 1)
                                for j in range(CHUNKS):
                                    pool.indirect_dma_start(
                                        rows[:, r, j, :], None, h_dram[:, :],
                                        bass.IndirectOffsetOnAxis(ap=src_idx[:, r, j:j + 1], axis=0),
                                    ).then_inc(gathered[r], 16)
                        if with_features:
                            for r in range(FULL % RING, RING):
                                pool.memset(features[:, r, :, :], NEVER).then_inc(pad_set, 1)

                    @block.scalar
                    def _(act):
                        act.sem_inc(multiplied, RING)
                        with act.Fori(0, ROUNDS) as i:
                            for r in range(RING):
                                act.wait_ge(multiplied, i * RING + (r + 1))
                                table = edges[:, bass.ds(i * RING + r, 1), :, :].rearrange("p s a j -> p (s a) j")
                                act.activation(src_idx[:, r, :], table[:, 2, :], ACT.Copy).then_inc(idx_staged, 1)
                                act.activation(dst_w[:, r, :, :], table[:, 0:2, :], ACT.Copy).then_inc(dst_staged, 1)
                            if with_features:
                                for r in range(RING):
                                    act.wait_ge(summed, i * RING + (r + 1))
                                    act.activation(rows[:, r, :, :], rows[:, r, :, :], ACT.Relu)\
                                        .then_inc(messages_ready, 1)

                    @block.tensor
                    def _(pe):
                        with pe.Fori(0, ROUNDS) as i:
                            for r in range(RING):
                                pe.wait_ge(selected, i * RING + (r + 1))
                                pe.wait_ge(added, i * RING + (r + 1))
                                if with_features:
                                    pe.wait_ge(messages_ready, i * RING + (r + 1))
                                else:
                                    pe.wait_ge(gathered[r], i * (16 * CHUNKS) + 16 * CHUNKS)
                                for j in range(CHUNKS):
                                    last = pe.matmul(banks[r][0:D, 0:WINDOW], rows[:, r, j, :], select[:, r, j, :],
                                                     start=(j == 0), stop=(j == CHUNKS - 1))
                                last.then_inc(multiplied, 1)

                    @block.vector
                    def _(dve):
                        dve.sem_inc(added, RING)
                        with dve.Fori(0, ROUNDS) as i:
                            for r in range(RING):
                                dve.wait_ge(dst_staged, i * RING + (r + 1))
                                for j in range(CHUNKS):
                                    last = dve.tensor_scalar(
                                        select[:, r, j, :], iota_now[:, :], dst_w[:, r, 0, j:j + 1],
                                        None if with_features else dst_w[:, r, 1, j:j + 1],
                                        ALU.is_equal, ALU.bypass if with_features else ALU.mult)
                                last.then_inc(selected, 1)
                            if with_features:
                                for r in range(RING):
                                    dve.wait_ge(gathered[r], i * (16 * CHUNKS) + 16 * CHUNKS)
                                    dve.wait_ge(features_loaded[r], i * 16 + 16)
                                    dve.tensor_tensor(rows[:, r, :, :], rows[:, r, :, :], features[:, r, :, :],
                                                      ALU.add).then_inc(summed, 1)
                            for r in range(RING):
                                dve.wait_ge(multiplied, i * RING + (RING + r + 1))
                                base = dve.value_load(base_now[0:1, bass.ds(i * RING + r, 1)],
                                                      min_val=0, max_val=N - 1)
                                window = acc[:, bass.ds(base, WINDOW)]
                                dve.wait_ge(added, i * RING + (RING + r))
                                dve.tensor_tensor(window, window, banks[r][0:D, 0:WINDOW], ALU.add)\
                                    .then_inc(added, 1)

                    if with_features:
                        @block.sync
                        def _(sp):
                            wide = edge_attr[0:FULL * SUPER, :].rearrange("(s p j) d -> s p j d", p=P, j=CHUNKS)
                            whole = FULL // RING
                            with sp.Fori(0, whole) as i:
                                for r in range(RING):
                                    sp.wait_ge(multiplied, i * RING + (r + 1))
                                    sp.dma_start(features[:, r, :, :], wide[bass.ds(i * RING + r, 1), :, :, :]
                                                 .rearrange("s p j d -> (s p) j d")).then_inc(features_loaded[r], 16)
                            for r in range(RING):
                                slot = features[:, r, :, :]
                                if r < FULL % RING:
                                    sp.wait_ge(multiplied, whole * RING + r + 1)
                                    sp.dma_start(slot, wide[whole * RING + r, :, :, :]).then_inc(features_loaded[r], 16)
                                    continue
                                sp.wait_ge(pad_set, r - FULL % RING + 1)
                                if r == FULL % RING:
                                    e0, e1 = FULL * SUPER, FULL * SUPER + REST_P * CHUNKS
                                    sp.dma_start(slot[0:REST_P, :, :], edge_attr[e0:e1, :]
                                                 .rearrange("(p j) d -> p j d", j=CHUNKS)).then_inc(part_loaded, 16)
                                    sp.dma_start(slot[REST_P:REST_P + 1, 0:REST_J, :], edge_attr[e1:E, :]
                                                 .rearrange("(p j) d -> p j d", p=1)).then_inc(part_loaded, 16)
                                    sp.wait_ge(part_loaded, 32)
                                sp.sem_inc(features_loaded[r], 16)

                with nc.Block() as block:
                    @block.vector
                    def _(dve):
                        dve.tensor_scalar(iota_now[:, :], iota_now[:, :], float(WINDOW), None, ALU.add)
                        dve.tensor_scalar(base_now[:, :], base_now[:, :], float(WINDOW), float(NP),
                                          ALU.add, ALU.min)

                    @block.gpsimd
                    def _(pool):
                        pool.dma_reset(range(gathered[0].num, gathered[-1].num + 1))
                        for signal in in_round:
                            pool.sem_clear(signal)

        prepare()
        widest = nc.values_load(span_max[0:1, 0:1], min_val=0, max_val=N - 1)
        update("first", first=True)
        edge_sum()
        update("project")
        edge_sum()
        update("add")
        edge_sum()
        update("hop")
        edge_sum()
        update("add")
        edge_sum(with_features=True)
        update("last")


def kernel(x, src, dst, edge_attr_48, edge_weight, L0_gnn_w, L0_gnn_b, L3_gnn_eps):
    import numpy as np
    import concourse.bacc as bacc
    from concourse import mybir
    from concourse.bass_utils import run_bass_kernel_spmd

    nc = bacc.Bacc("TRN2", target_bir_lowering=False, num_devices=1)
    given = {"x": x, "src": src, "dst": dst, "edge_attr": edge_attr_48, "edge_weight": edge_weight,
             "weight": L0_gnn_w, "bias": L0_gnn_b, "eps": L3_gnn_eps}
    arrays = {name: np.ascontiguousarray(a) for name, a in given.items()}
    aps = [nc.dram_tensor(name, a.shape, mybir.dt.from_np(a.dtype), kind="ExternalInput").ap()
           for name, a in arrays.items()]
    out = nc.dram_tensor("out", x.shape, mybir.dt.float32, kind="ExternalOutput").ap()
    gnn_kernel(nc, *aps, out)
    result = run_bass_kernel_spmd(nc, [arrays], core_ids=[0])
    return result.results[0]["out"]
```

```python
import concourse.bass as bass
from concourse import mybir
from contextlib import ExitStack


def gnn_kernel(nc, x, src, dst, edge_attr, edge_weight, weight, bias, eps, out):
    fp32, int32, int16 = mybir.dt.float32, mybir.dt.int32, mybir.dt.int16
    ALU, ACT, AX = mybir.AluOpType, mybir.ActivationFunctionType, mybir.AxisListType

    N, D = x.shape
    E = src.shape[0]
    P = 128
    CHUNKS = 8
    SUPER = CHUNKS * P
    WINDOW_BITS = 6
    WINDOW = 1 << WINDOW_BITS
    RING = 4
    ROUNDS = -(-E // (SUPER * RING))
    S = ROUNDS * RING
    FULL, REST = divmod(E, SUPER)
    REST_P, REST_J = divmod(REST, CHUNKS)
    GROUPS = -(-S // P)
    HALF = CHUNKS // 2
    LOW_BITS = 3
    LOW = 1 << LOW_BITS
    PIECES = 14
    T = PIECES * LOW
    Q = -(-N // T)
    NP = Q * T
    LAST_P, LAST_T = divmod(N, T)
    LAST_P16 = LAST_P // 16 * 16
    ACC = NP + WINDOW
    PER_BANK = 512 // D
    LN_EPS = 1e-5
    NEVER = -1.0e38

    DENSE_GROUPS = 2
    WIDE = 224
    TILES = 18
    FIRST_ROUND = DENSE_GROUPS * P // RING
    MIDDLES = [(2 * g + 1) * P * SUPER * N // (2 * E) for g in range(DENSE_GROUPS)]
    START = [max(0, m - TILES * WIDE // 2) for m in MIDDLES]
    APART = 127
    PIECE = WIDE * LOW
    SLOTS = 7
    EVEN_BITS = (PIECE & -PIECE).bit_length() - 1
    SOURCE_LINES = Q * PIECES
    assert S // RING - FIRST_ROUND > DENSE_GROUPS * TILES and PIECES % SLOTS == 0
    assert TILES * SOURCE_LINES * (PIECE >> EVEN_BITS) < 1 << 24
    assert E > DENSE_GROUPS * P * SUPER + APART

    FILLS = 7

    h_dram = nc.dram_tensor("h_rows", [NP, D], fp32).ap()
    h_tiles = h_dram.rearrange("(p t) d -> p t d", t=T)
    dense = [nc.dram_tensor(f"dense{g}", [TILES * SOURCE_LINES * PIECE, 1], fp32).ap()
             for g in range(DENSE_GROUPS)]
    dense_fills = [m.rearrange("(t p a f) o -> t a p (f o)", t=TILES, p=Q, a=FILLS) for m in dense]
    dense_pieces = [m.rearrange("(t p b f) o -> t b p (f o)", t=TILES, p=Q, b=PIECES) for m in dense]

    ctx = ExitStack()
    with ctx:
        def sb(name, shape, dt=fp32):
            return ctx.enter_context(nc.sbuf_tensor(name, shape, dt))

        edge_w = sb("edge_w", [P, S, CHUNKS])
        edge_ends = sb("edge_ends", [P, S, 2, CHUNKS], int16)
        place = sb("place", [P, DENSE_GROUPS, P, CHUNKS], int32)
        place_w = sb("place_w", [P, DENSE_GROUPS, P, CHUNKS])
        base_row = sb("base_row", [1, S], int32)
        verdict = sb("verdict", [1, 4 * GROUPS])
        sorted_enough = sb("sorted_enough", [1, 1], int32)
        span_max = sb("span_max", [1, 1], int32)
        iota = sb("iota", [P, WINDOW])
        ident = sb("ident", [P, P])
        w_sb = sb("w_sb", [D, D])
        bias_sb = sb("bias_sb", [P, D])
        eps_sb = sb("eps_sb", [P, 1])
        x_sb = sb("x_sb", [Q, T, D])
        h_sb = sb("h_sb", [Q, T, D])
        acc = sb("acc", [D, ACC])
        iota_now = sb("iota_now", [P, WINDOW])
        base_now = sb("base_now", [1, S], int32)
        arena = sb("arena", [P, SLOTS * PIECE])
        scratch = arena[0:Q, 0:T * D].rearrange("p (t d) -> p t d", d=D)
        pieces = arena[:, :].rearrange("p (b f) -> p b f", b=SLOTS)
        features = arena[:, 0:RING * CHUNKS * D].rearrange("p (r j d) -> p r j d", r=RING, j=CHUNKS)

        def sem(name):
            return ctx.enter_context(nc.semaphore(name))

        banks = [ctx.enter_context(nc.psum_tensor(f"bank{i}", [P, 512], fp32)) for i in range(8)]

        def group_rows(g):
            n = min(P, S - g * P)
            return n, max(0, min(n, FULL - g * P))

        def prepare():
            LONG = SUPER + P
            cut = [0]

            def part(n, dt=fp32, rows=P):
                cut[0] += n
                return arena[0:rows, cut[0] - n:cut[0]].bitcast(dt)

            raw_src, raw_dst = part(SUPER, int32), part(LONG, int32)
            flat_dst, flat_w, flat_src = part(LONG), part(SUPER), part(SUPER)
            line, low, high = part(SUPER, int32), part(SUPER, int32), part(SUPER, int32)
            apart, over = part(SUPER), part(SUPER)
            iota_int = part(WINDOW, int32)
            base_float, span_row, order_row = part(S, rows=1), part(S, rows=1), part(S, rows=1)
            ends = part(4)
            assert cut[0] <= SLOTS * PIECE
            turned = [banks[i][:, 0:HALF * P].rearrange("p (j s) -> p j s", j=HALF) for i in range(2)]
            turned_ends = banks[2][:, 0:3 * P].rearrange("p (i s) -> p i s", i=3)
            const_ready, pool_step = sem("const_ready"), sem("pool_step")
            raw_loaded, w_loaded = sem("raw_loaded"), sem("w_loaded")
            ends_padded, w_padded, w_used = sem("ends_padded"), sem("w_padded"), sem("w_used")
            flat_ready, dve_step = sem("flat_ready"), sem("dve_step")
            turned_ready, turned_used = sem("turned_ready"), [sem("turned_used0"), sem("turned_used1")]
            ends_turned, ends_used, raw_used = sem("ends_turned"), sem("ends_used"), sem("raw_used")
            x_pad_set, x_loaded, small_loaded = sem("x_pad_set"), sem("x_loaded"), sem("small_loaded")

            assert group_rows(GROUPS - 1)[1] < group_rows(GROUPS - 1)[0] <= P < S and DENSE_GROUPS < GROUPS

            def w_loads(g):
                return 16 * sum((full > 0) + (full < n and REST > 0)
                                for n, full in map(group_rows, range(g + 1)))

            with nc.Block() as block:
                @block.gpsimd
                def _(pool):
                    pool.memset(x_sb[:, :, :], 0.0).then_inc(x_pad_set, 1)
                    pool.iota(iota_int, pattern=[[1, WINDOW]], base=0, channel_multiplier=0)\
                        .then_inc(pool_step, 1)
                    pool.memset(ident[:, :], 0.0).then_inc(pool_step, 1)
                    pool.wait_ge(pool_step, 2)
                    pool.tensor_copy(iota[:, :], iota_int).then_inc(const_ready, 1)
                    pool.affine_select(out=ident[:, :], in_=ident[:, :], compare_op=ALU.not_equal,
                                       fill=1.0, base=0, pattern=[[-1, P]], channel_multiplier=1)\
                        .then_inc(const_ready, 1)
                    pool.memset(acc[:, :], 0.0).then_inc(const_ready, 1)
                    pool.wait_ge(raw_used, GROUPS - 1)
                    pool.memset(raw_src, 0).then_inc(ends_padded, 1)
                    pool.memset(raw_dst, N - 1).then_inc(ends_padded, 1)
                    pool.wait_ge(turned_ready, 6 * (GROUPS - 1) - 2)
                    pool.wait_ge(w_used, GROUPS - 1)
                    pool.memset(flat_w, 0.0).then_inc(w_padded, 1)

                @block.sync
                def _(sp):
                    for g in range(GROUPS):
                        n, full = group_rows(g)
                        e0 = g * P * SUPER
                        if full < n:
                            sp.wait_ge(ends_padded, 2)
                        elif g > 0:
                            sp.wait_ge(raw_used, g)
                        for a, rows_in, loaded in ((dst, raw_dst, raw_loaded), (src, raw_src, raw_loaded),
                                                   (edge_weight, flat_w, w_loaded)):
                            if rows_in is raw_src and g < DENSE_GROUPS:
                                sp.dma_start(raw_dst[:, SUPER:LONG], dst[e0 + SUPER:e0 + SUPER + P * SUPER]
                                             .rearrange("(s e) -> s e", e=SUPER)[:, 0:P])\
                                    .then_inc(raw_loaded, 16)
                            if rows_in is flat_w and g > 0:
                                if full < n:
                                    sp.wait_ge(w_padded, 1)
                                else:
                                    sp.wait_ge(w_used, g)
                                    sp.wait_ge(turned_ready, 6 * g - 2)
                            if full:
                                sp.dma_start(rows_in[0:full, 0:SUPER], a[e0:e0 + full * SUPER]
                                             .rearrange("(s e) -> s e", e=SUPER)).then_inc(loaded, 16)
                            if full < n and REST:
                                sp.dma_start(rows_in[full:full + 1, 0:REST], a[FULL * SUPER:E]
                                             .rearrange("(s e) -> s e", s=1)).then_inc(loaded, 16)

                @block.scalar
                def _(act):
                    act.dma_start(w_sb[:, :], weight).then_inc(small_loaded, 16)
                    act.dma_start(bias_sb[:, :], bias.rearrange("(a d) -> a d", a=1)
                                  .to_broadcast([P, D])).then_inc(small_loaded, 16)
                    act.dma_start(eps_sb[:, :], eps.rearrange("(a d) -> a d", a=1)
                                  .to_broadcast([P, 1])).then_inc(small_loaded, 16)
                    act.wait_ge(x_pad_set, 1)
                    for p0, p1 in ((0, LAST_P16), (LAST_P16, LAST_P)):
                        act.dma_start(x_sb[p0:p1, :, :], x[p0 * T:p1 * T, :]
                                      .rearrange("(p t) d -> p t d", t=T)).then_inc(x_loaded, 16)
                    act.dma_start(x_sb[LAST_P:LAST_P + 1, 0:LAST_T, :], x[LAST_P * T:N, :]
                                  .rearrange("(p t) d -> p t d", p=1)).then_inc(x_loaded, 16)
                    for g in range(GROUPS):
                        n, _full = group_rows(g)
                        s0, s1 = g * P, g * P + n
                        for a, table in enumerate((edge_ends[:, s0:s1, 0, HALF:], edge_w[:, s0:s1, HALF:],
                                                   edge_ends[:, s0:s1, 1, HALF:])):
                            act.wait_ge(turned_ready, 6 * g + 2 * a + 2)
                            act.activation(table, turned[1][:, :, 0:n].rearrange("p j s -> p s j"),
                                           ACT.Copy).then_inc(turned_used[1], 1)
                    act.wait_ge(small_loaded, 48)
                    act.wait_ge(x_loaded, 48)

                @block.tensor
                def _(pe):
                    pe.wait_ge(const_ready, 3)
                    for g in range(GROUPS):
                        n, _full = group_rows(g)
                        pe.wait_ge(flat_ready, g + 1)
                        if g > 0:
                            pe.wait_ge(ends_used, g)
                        for i in range(3):
                            last = pe.transpose(turned_ends[0:1, i, 0:n], ends[0:n, i:i + 1], ident[0:n, 0:n])
                        last.then_inc(ends_turned, 1)
                        for a, flat in enumerate((flat_dst, flat_w, flat_src)):
                            if flat is flat_w:
                                pe.wait_ge(w_loaded, w_loads(g))
                            row = flat[0:n, 0:SUPER].rearrange("s (p j) -> s j p", j=CHUNKS)
                            for half in range(2):
                                if 3 * g + a > 0:
                                    pe.wait_ge(turned_used[half], 3 * g + a)
                                for j in range(HALF):
                                    last = pe.transpose(turned[half][:, j, 0:n],
                                                        row[:, HALF * half + j, :], ident[0:n, 0:n])
                                last.then_inc(turned_ready, 1)

                @block.vector
                def _(dve):
                    steps = [0]

                    def step(instruction):
                        steps[0] += 1
                        instruction.then_inc(dve_step, 1)
                        dve.wait_ge(dve_step, steps[0])

                    dve.memset(ends, 0.0)
                    loads = 0
                    for g in range(GROUPS):
                        n, full = group_rows(g)
                        if g > 0:
                            dve.wait_ge(turned_ready, 6 * g)
                        loads += 2 * ((full > 0) + (full < n and REST > 0)) + (g < DENSE_GROUPS)
                        dve.wait_ge(raw_loaded, 16 * loads)
                        width = LONG if g < DENSE_GROUPS else SUPER
                        step(dve.tensor_copy(flat_src[0:n, :], raw_src[0:n, :]))
                        step(dve.tensor_copy(flat_dst[0:n, 0:width], raw_dst[0:n, 0:width]))
                        if g < DENSE_GROUPS:
                            step(dve.tensor_tensor(apart, flat_dst[:, 1:SUPER + 1], flat_dst[:, 0:SUPER],
                                                   ALU.subtract))
                            step(dve.tensor_reduce(ends[:, 2:3], apart, AX.X, ALU.min))
                            step(dve.scalar_tensor_tensor(apart, flat_dst[:, APART:SUPER + APART], -1.0,
                                                          flat_dst[:, 0:SUPER], ALU.add, ALU.subtract))
                            step(dve.tensor_reduce(ends[:, 3:4], apart, AX.X, ALU.min))
                            step(dve.tensor_tensor(ends[:, 2:3], ends[:, 2:3], ends[:, 3:4], ALU.min))
                        step(dve.tensor_reduce(ends[0:n, 0:1], flat_dst[0:n, 0:SUPER], AX.X, ALU.min))
                        step(dve.tensor_scalar(flat_dst[0:n, 0:SUPER], flat_dst[0:n, 0:SUPER],
                                               ends[0:n, 0:1], None, ALU.subtract))
                        dve.tensor_reduce(ends[0:n, 1:2], flat_dst[0:n, 0:SUPER], AX.X, ALU.max)\
                            .then_inc(flat_ready, 1)
                        if g < DENSE_GROUPS:
                            ints = raw_dst[:, 0:SUPER]
                            step(dve.tensor_scalar(ints, ints, -float(START[g]), None, ALU.add))
                            step(dve.tensor_scalar(line, ints, 1.0 / WIDE, None, ALU.mult))
                            step(dve.scalar_tensor_tensor(over, line, -float(WIDE), ints, ALU.mult, ALU.add))
                            step(dve.tensor_scalar(apart, over, 0.0, None, ALU.is_lt))
                            step(dve.tensor_tensor(line, line, apart, ALU.subtract))
                            step(dve.scalar_tensor_tensor(over, apart, float(WIDE), over, ALU.mult, ALU.add))
                            step(dve.tensor_scalar(high, raw_src, LOW_BITS, None, ALU.logical_shift_right))
                            step(dve.scalar_tensor_tensor(line, line, float(SOURCE_LINES), high,
                                                          ALU.mult, ALU.add))
                            step(dve.tensor_scalar(line, line, float(PIECE >> EVEN_BITS), None, ALU.mult))
                            step(dve.tensor_scalar(line, line, EVEN_BITS, None, ALU.logical_shift_left))
                            step(dve.tensor_scalar(low, raw_src, LOW - 1, None, ALU.bitwise_and))
                            step(dve.scalar_tensor_tensor(low, over, float(LOW), low, ALU.mult, ALU.add))
                            step(dve.tensor_tensor(line, line, low, ALU.add))
                        dve.sem_inc(raw_used, 1)
                        if g < DENSE_GROUPS:
                            dve.wait_ge(w_loaded, w_loads(g))

                            def by_place(table):
                                return table.rearrange("p (q m) -> p q m", q=CHUNKS)
                            step(dve.tensor_scalar(place[:, g, :, :].rearrange("p m q -> p q m"),
                                                   by_place(line), 0, None, ALU.bitwise_or))
                            step(dve.tensor_copy(place_w[:, g, :, :].rearrange("p m q -> p q m"),
                                                 by_place(flat_w)))
                        dve.sem_inc(w_used, 1)
                        dve.wait_ge(ends_turned, g + 1)
                        s0, s1 = g * P, g * P + n
                        step(dve.tensor_copy(base_float[:, s0:s1], turned_ends[0:1, 0, 0:n]))
                        step(dve.tensor_copy(span_row[:, s0:s1], turned_ends[0:1, 1, 0:n]))
                        step(dve.tensor_copy(order_row[:, s0:s1], turned_ends[0:1, 2, 0:n]))
                        dve.sem_inc(ends_used, 1)
                        for a, table in enumerate((edge_ends[:, s0:s1, 0, 0:HALF], edge_w[:, s0:s1, 0:HALF],
                                                   edge_ends[:, s0:s1, 1, 0:HALF])):
                            dve.wait_ge(turned_ready, 6 * g + 2 * a + 1)
                            dve.tensor_copy(table, turned[0][:, :, 0:n].rearrange("p j s -> p s j"))\
                                .then_inc(turned_used[0], 1)
                    step(dve.tensor_copy(base_row[:, :], base_float))
                    step(dve.tensor_reduce(span_max[0:1, 0:1], span_row, AX.X, ALU.max))
                    step(dve.memset(verdict[:, :], 0.0))
                    step(dve.tensor_reduce(verdict[:, 0:1], span_row, AX.X, ALU.max))
                    step(dve.tensor_scalar(verdict[:, 0:1], verdict[:, 0:1], -1.0, WINDOW - 1.0,
                                           ALU.mult, ALU.add))
                    step(dve.tensor_tensor(span_row, span_row, base_float, ALU.add))
                    for g in range(DENSE_GROUPS):
                        of_group = slice(g * P, g * P + P)
                        order, least, most = (verdict[:, 1 + 3 * g + i:2 + 3 * g + i] for i in range(3))
                        step(dve.tensor_reduce(order, order_row[:, of_group], AX.X, ALU.min))
                        step(dve.tensor_reduce(least, base_float[:, of_group], AX.X, ALU.min))
                        step(dve.tensor_scalar(least, least, -float(START[g]), None, ALU.add))
                        step(dve.tensor_reduce(most, span_row[:, of_group], AX.X, ALU.max))
                        step(dve.tensor_scalar(most, most, -1.0, START[g] + TILES * WIDE - 1.0,
                                               ALU.mult, ALU.add))
                    step(dve.tensor_reduce(order_row[:, 0:1], verdict[:, :], AX.X, ALU.min))
                    step(dve.tensor_scalar(sorted_enough[:, :], order_row[:, 0:1], 0.0, None, ALU.is_ge))

        stats = arena[0:Q, T * D:T * (D + 3)].rearrange("p (k t) -> p k t", k=3)
        acc_turned, acc_used, up_step = sem("acc_turned"), sem("acc_used"), sem("up_step")
        centred, squared = sem("centred"), sem("squared")
        var_ready, std_ready = sem("var_ready"), sem("std_ready")
        rows_ready, rows_stored = sem("rows_ready"), sem("rows_stored")
        in_update = [acc_turned, acc_used, up_step, centred, squared, var_ready, std_ready, rows_ready,
                     rows_stored]

        def update(kind, first=False):
            PARTS = 2
            cuts = [T * i // PARTS for i in range(PARTS + 1)]
            tiles = [(t, min(t + PER_BANK, cuts[i + 1])) for i in range(PARTS)
                     for t in range(cuts[i], cuts[i + 1], PER_BANK)]
            norm = kind != "hop" and kind != "last"
            with nc.Block() as block:
                if not first:
                    @block.tensor
                    def _(pe):
                        for i, (t0, t1) in enumerate(tiles):
                            if i >= 4:
                                pe.wait_ge(acc_used, i - 3)
                            for t in range(t0, t1):
                                turned = banks[4 + i % 4][0:Q, (t - t0) * D:(t - t0 + 1) * D]
                                column = acc[:, t:t + (Q - 1) * T + 1:T]
                                if kind == "project":
                                    last = pe.matmul(turned, column, w_sb[:, :], start=True, stop=True)
                                else:
                                    last = pe.transpose(turned, column, ident[0:D, 0:D])
                            last.then_inc(acc_turned, 1)


                if kind != "last":
                    @block.gpsimd
                    def _(pool):
                        pool.tensor_copy(iota_now[:, :], iota[:, :])
                        pool.tensor_copy(base_now[:, :], base_row[:, :])
                        if not first:
                            pool.wait_ge(acc_turned, len(tiles))
                            pool.memset(acc[:, :], 0.0)

                @block.vector
                def _(dve):
                    steps = [0]

                    def step(instruction):
                        steps[0] += 1
                        instruction.then_inc(up_step, 1)
                        dve.wait_ge(up_step, steps[0])

                    if kind == "last":
                        step(dve.tensor_scalar(eps_sb[:, :], eps_sb[:, :], 1.0, None, ALU.add))
                        step(dve.scalar_tensor_tensor(x_sb[:, :, :], h_sb[:, :, :], eps_sb[0:Q, 0:1],
                                                      x_sb[:, :, :], ALU.mult, ALU.add))
                    i = 0
                    for part in range(PARTS):
                        c0, c1 = cuts[part], cuts[part + 1]
                        while not first and i < len(tiles) and tiles[i][0] < c1:
                            t0, t1 = tiles[i]
                            new = banks[4 + i % 4][0:Q, 0:(t1 - t0) * D].rearrange("p (t d) -> p t d", d=D)
                            xs = x_sb[:, t0:t1, :]
                            dve.wait_ge(acc_turned, i + 1)
                            if kind == "project":
                                step(dve.tensor_tensor(scratch[:, t0:t1, :], new, bias_sb[0:Q, :].unsqueeze(1)
                                                       .to_broadcast([Q, t1 - t0, D]), ALU.add))
                                dve.sem_inc(acc_used, 1)
                                step(dve.scalar_tensor_tensor(xs, scratch[:, t0:t1, :], 0.0, xs,
                                                              ALU.max, ALU.add))
                            elif kind == "hop":
                                step(dve.tensor_copy(h_sb[:, t0:t1, :], new))
                                dve.sem_inc(acc_used, 1)
                            else:
                                step(dve.tensor_tensor(xs, new, xs, ALU.add))
                                dve.sem_inc(acc_used, 1)
                            i += 1
                        if norm:
                            xs, hs = x_sb[:, c0:c1, :], h_sb[:, c0:c1, :]
                            total, mean, var = (stats[:, k, c0:c1] for k in range(3))
                            wide = [Q, c1 - c0, D]
                            step(dve.tensor_reduce(total, xs, AX.X, ALU.add))
                            step(dve.tensor_scalar(mean, total, 1.0 / D, None, ALU.mult))
                            dve.tensor_tensor(hs, xs, mean.unsqueeze(2).to_broadcast(wide), ALU.subtract)\
                                .then_inc(centred, 1)
                        else:
                            dve.sem_inc(rows_ready, 1)
                    if norm:
                        for part in range(PARTS):
                            c0, c1 = cuts[part], cuts[part + 1]
                            _total, _mean, var = (stats[:, k, c0:c1] for k in range(3))
                            dve.wait_ge(squared, part + 1)
                            step(dve.tensor_reduce(var, scratch[:, c0:c1, :], AX.X, ALU.add))
                            dve.tensor_scalar(var, var, 1.0 / D, LN_EPS, ALU.mult, ALU.add).then_inc(var_ready, 1)
                        for part in range(PARTS):
                            c0, c1 = cuts[part], cuts[part + 1]
                            hs = h_sb[:, c0:c1, :]
                            std, inverse, _var = (stats[:, k, c0:c1] for k in range(3))
                            dve.wait_ge(std_ready, part + 1)
                            step(dve.reciprocal(inverse, std))
                            dve.scalar_tensor_tensor(hs, hs, 0.0, inverse.unsqueeze(2)
                                                     .to_broadcast([Q, c1 - c0, D]),
                                                     ALU.max, ALU.mult).then_inc(rows_ready, 1)

                if norm:
                    @block.scalar
                    def _(act):
                        for part in range(PARTS):
                            c0, c1 = cuts[part], cuts[part + 1]
                            act.wait_ge(centred, part + 1)
                            act.activation(scratch[:, c0:c1, :], h_sb[:, c0:c1, :], ACT.Square)\
                                .then_inc(squared, 1)
                        for part in range(PARTS):
                            c0, c1 = cuts[part], cuts[part + 1]
                            act.wait_ge(var_ready, part + 1)
                            act.activation(stats[:, 0, c0:c1], stats[:, 2, c0:c1], ACT.Sqrt)\
                                .then_inc(std_ready, 1)

                @block.sync
                def _(sp):
                    for part in range(PARTS):
                        c0, c1 = cuts[part], cuts[part + 1]
                        sp.wait_ge(rows_ready, part + 1)
                        if kind != "last":
                            sp.dma_start(h_tiles[:, c0:c1, :], h_sb[:, c0:c1, :]).then_inc(rows_stored, 16)
                        else:
                            for p0, p1 in ((0, LAST_P16), (LAST_P16, LAST_P)):
                                sp.dma_start(out[p0 * T:p1 * T, :].rearrange("(p t) d -> p t d", t=T)
                                             [:, c0:c1, :], x_sb[p0:p1, c0:c1, :]).then_inc(rows_stored, 16)
                            c1 = min(c1, LAST_T)
                            sp.dma_start(out[LAST_P * T:N, :].rearrange("(p t) d -> p t d", p=1)
                                         [:, c0:c1, :], x_sb[LAST_P:LAST_P + 1, c0:c1, :]).then_inc(rows_stored, 16)
                    sp.wait_ge(rows_stored, 16 * PARTS * (3 if kind == "last" else 1))

            with nc.Block() as block:
                @block.gpsimd
                def _(pool):
                    for signal in in_update:
                        pool.sem_clear(signal)

        src_idx = sb("src_idx", [P, RING, CHUNKS], int32)
        dst_w = sb("dst_w", [P, RING, 2, CHUNKS])
        rows = sb("rows", [P, RING, CHUNKS, D])
        SELECTS = 2
        select = sb("select", [P, SELECTS, CHUNKS, WINDOW])
        idx_staged, dst_staged = sem("idx_staged"), sem("dst_staged")
        gathered = [sem(f"gathered{r}") for r in range(RING)]
        selected, multiplied, added = sem("selected"), sem("multiplied"), sem("added")
        features_loaded = [sem(f"features_loaded{r}") for r in range(RING)]
        summed, messages_ready = sem("summed"), sem("messages_ready")
        pad_set, begun, part_loaded = sem("pad_set"), sem("begun"), sem("part_loaded")
        in_round = [idx_staged, dst_staged, *gathered, selected, multiplied, added, *features_loaded,
                    summed, messages_ready, pad_set, begun, part_loaded]

        def stage_edges(act, i, r, first):
            s = bass.ds(i * RING + (first + r), 1)
            act.activation(src_idx[:, r, :], edge_ends[:, s, 1, :].rearrange("p s j -> p (s j)"),
                           ACT.Copy).then_inc(idx_staged, 1)
            act.activation(dst_w[:, r, 0, :], edge_ends[:, s, 0, :].rearrange("p s j -> p (s j)"),
                           ACT.Copy).then_inc(dst_staged, 1)
            act.activation(dst_w[:, r, 1, :], edge_w[:, s, :].rearrange("p s j -> p (s j)"),
                           ACT.Copy).then_inc(dst_staged, 1)

        def stage_next(act, i, r, first):
            act.wait_ge(gathered[r], i * (16 * CHUNKS) + 16 * CHUNKS)
            act.wait_ge(selected, i * RING + (r + 1))
            stage_edges(act, i + 1, r, first)

        def gather(pool, i, r):
            pool.wait_ge(idx_staged, i * RING + (r + 1))
            pool.wait_ge(multiplied, i * RING + (r + 1))
            pool.sem_inc(begun, 1)
            for j in range(CHUNKS):
                pool.indirect_dma_start(
                    rows[:, r, j, :], None, h_dram[:, :],
                    bass.IndirectOffsetOnAxis(ap=src_idx[:, r, j:j + 1], axis=0),
                ).then_inc(gathered[r], 16)

        def select_destinations(dve, i, r, weighted=True):
            dve.wait_ge(dst_staged, i * (2 * RING) + 2 * (r + 1))
            dve.wait_ge(multiplied, i * RING + (RING - SELECTS + r + 1))
            for j in range(CHUNKS):
                last = dve.tensor_scalar(
                    select[:, r % SELECTS, j, :], iota_now[:, :], dst_w[:, r, 0, j:j + 1],
                    dst_w[:, r, 1, j:j + 1] if weighted else None,
                    ALU.is_equal, ALU.mult if weighted else ALU.bypass)
            last.then_inc(selected, 1)

        def multiply(pe, i, r, features_too=False):
            pe.wait_ge(selected, i * RING + (r + 1))
            pe.wait_ge(added, i * RING + (r + 1))
            if features_too:
                pe.wait_ge(messages_ready, i * RING + (r + 1))
            else:
                pe.wait_ge(gathered[r], i * (16 * CHUNKS) + 16 * CHUNKS)
            for j in range(CHUNKS):
                last = pe.matmul(banks[r][0:D, 0:WINDOW], rows[:, r, j, :], select[:, r % SELECTS, j, :],
                                 start=(j == 0), stop=(j == CHUNKS - 1))
            last.then_inc(multiplied, 1)

        def add_window(dve, i, r, first, before=None):
            dve.wait_ge(multiplied, i * RING + (RING + r + 1))
            base = dve.value_load(base_now[0:1, bass.ds(i * RING + (first + r), 1)], min_val=0, max_val=NP)
            window = acc[:, bass.ds(base, WINDOW)]
            dve.wait_ge(added, i * RING + (RING + r))
            if before is not None:
                dve.wait_ge(*before)
            dve.tensor_tensor(window, window, banks[r][0:D, 0:WINDOW], ALU.add).then_inc(added, 1)

        def edge_sum(with_features=False):
            with nc.Fori(0, (widest >> WINDOW_BITS) + 1):
                with nc.Block() as block:
                    @block.gpsimd
                    def _(pool):
                        with pool.Fori(0, ROUNDS) as i:
                            for r in range(RING):
                                gather(pool, i, r)
                        if with_features:
                            for r in range(FULL % RING, RING):
                                pool.memset(features[:, r, :, :], NEVER).then_inc(pad_set, 1)

                    @block.scalar
                    def _(act):
                        def message(i, r):
                            if with_features:
                                act.wait_ge(summed, i * RING + (r + 1))
                                act.activation(rows[:, r, :, :], rows[:, r, :, :], ACT.Relu)\
                                    .then_inc(messages_ready, 1)

                        for r in range(RING):
                            stage_edges(act, 0, r, 0)
                        with act.Fori(0, ROUNDS - 1) as i:
                            for r in range(RING):
                                message(i, r)
                                stage_next(act, i, r, 0)
                        for r in range(RING):
                            message(ROUNDS - 1, r)

                    @block.tensor
                    def _(pe):
                        pe.sem_inc(multiplied, RING)
                        with pe.Fori(0, ROUNDS) as i:
                            for r in range(RING):
                                multiply(pe, i, r, with_features)

                    @block.vector
                    def _(dve):
                        dve.sem_inc(added, RING)
                        with dve.Fori(0, ROUNDS) as i:
                            for r in range(RING + SELECTS - 1):
                                if r < RING:
                                    select_destinations(dve, i, r, not with_features)
                                if r < RING and with_features:
                                    dve.wait_ge(gathered[r], i * (16 * CHUNKS) + 16 * CHUNKS)
                                    dve.wait_ge(features_loaded[r], i * 16 + 16)
                                    dve.tensor_tensor(rows[:, r, :, :], rows[:, r, :, :], features[:, r, :, :],
                                                      ALU.add).then_inc(summed, 1)
                                if r >= SELECTS - 1:
                                    add_window(dve, i, r - (SELECTS - 1), 0)

                    if with_features:
                        @block.sync
                        def _(sp):
                            wide = edge_attr[0:FULL * SUPER, :].rearrange("(s p j) d -> s p j d", p=P, j=CHUNKS)
                            whole = FULL // RING
                            with sp.Fori(0, whole) as i:
                                for r in range(RING):
                                    sp.wait_ge(multiplied, i * RING + (r + 1))
                                    sp.dma_start(features[:, r, :, :], wide[bass.ds(i * RING + r, 1), :, :, :]
                                                 .rearrange("s p j d -> (s p) j d")).then_inc(features_loaded[r], 16)
                            for r in range(RING):
                                slot = features[:, r, :, :]
                                if r < FULL % RING:
                                    sp.wait_ge(multiplied, whole * RING + r + 1)
                                    sp.dma_start(slot, wide[whole * RING + r, :, :, :]).then_inc(features_loaded[r], 16)
                                    continue
                                sp.wait_ge(pad_set, r - FULL % RING + 1)
                                if r == FULL % RING:
                                    e0, e1 = FULL * SUPER, FULL * SUPER + REST_P * CHUNKS
                                    sp.dma_start(slot[0:REST_P, :, :], edge_attr[e0:e1, :]
                                                 .rearrange("(p j) d -> p j d", j=CHUNKS)).then_inc(part_loaded, 16)
                                    sp.dma_start(slot[REST_P:REST_P + 1, 0:REST_J, :], edge_attr[e1:E, :]
                                                 .rearrange("(p j) d -> p j d", p=1)).then_inc(part_loaded, 16)
                                    sp.wait_ge(part_loaded, 32)
                                sp.sem_inc(features_loaded[r], 16)

                with nc.Block() as block:
                    @block.vector
                    def _(dve):
                        dve.tensor_scalar(iota_now[:, :], iota_now[:, :], float(WINDOW), None, ALU.add)
                        dve.tensor_scalar(base_now[:, :], base_now[:, :], float(WINDOW), float(NP),
                                          ALU.add, ALU.min)

                    @block.gpsimd
                    def _(pool):
                        pool.dma_reset(range(gathered[0].num, gathered[-1].num + 1))
                        for signal in in_round:
                            pool.sem_clear(signal)

        piece_loaded = [sem(f"piece_loaded{b}") for b in range(SLOTS)]
        piece_used, block_added = sem("piece_used"), sem("block_added")
        in_dense = [*piece_loaded, piece_used, block_added]
        LOADS = PIECES // SLOTS

        def load_block(sp, u, source):
            for b in range(PIECES):
                sp.wait_ge(piece_used, u * PIECES + (b + 1))
                sp.dma_start(pieces[0:Q, b % SLOTS, :], source[b, :, :]).then_inc(piece_loaded[b % SLOTS], 16)

        def multiply_block(pe, u, b0, b1):
            if b0 == 0:
                pe.wait_ge(block_added, u * 2 + 2)
            for b in range(b0, b1):
                pe.wait_ge(piece_loaded[b % SLOTS], u * (16 * LOADS) + 16 * (b // SLOTS + 1))
                piece = pieces[0:Q, b % SLOTS, :].rearrange("p (n l) -> p l n", l=LOW)
                for l in range(LOW):
                    half = 64 * (l % 2)
                    last = pe.matmul(banks[4][half:half + D, 0:WIDE], h_sb[:, b * LOW + l, :], piece[:, l, :],
                                     start=(b == 0 and l < 2), stop=(b == PIECES - 1 and l >= LOW - 2))
                last.then_inc(piece_used, 1)

        def add_block(dve, u, column, before=None):
            part = acc[:, bass.ds(column, WIDE)]
            dve.wait_ge(piece_used, u * PIECES + (SLOTS + PIECES))
            if before is not None:
                dve.wait_ge(*before)
            for half in range(2):
                dve.wait_ge(block_added, u * 2 + (half + 2))
                dve.tensor_tensor(part, part, banks[4][64 * half:64 * half + D, 0:WIDE], ALU.add)\
                    .then_inc(block_added, 1)

        def multiply_both(pe, i, u):
            for r in range(RING):
                multiply_block(pe, u, PIECES * r // RING, PIECES * (r + 1) // RING)
                multiply(pe, i, r)

        def add_both(dve, i, u, column):
            select_destinations(dve, i, 0)
            select_destinations(dve, i, 1)
            add_window(dve, i, 0, FIRST, before=(block_added, u * 2 + 2))
            select_destinations(dve, i, 2)
            add_window(dve, i, 1, FIRST)
            select_destinations(dve, i, 3)
            add_window(dve, i, 2, FIRST)
            add_block(dve, u, column, before=(added, i * RING + (RING + 3)))
            add_window(dve, i, 3, FIRST, before=(block_added, u * 2 + 4))

        def add_windows(dve, i):
            for r in range(RING + SELECTS - 1):
                if r < RING:
                    select_destinations(dve, i, r)
                if r >= SELECTS - 1:
                    add_window(dve, i, r - (SELECTS - 1), FIRST)

        def slots_start_free(engine):
            for signal, n in {nc.tensor: ((multiplied, RING), (piece_used, SLOTS)),
                              nc.vector: ((added, RING), (block_added, 2))}[engine]:
                engine.sem_inc(signal, n)

        def clear_dense(scattered=()):
            with nc.Block() as block:
                @block.gpsimd
                def _(pool):
                    pool.dma_reset(range(gathered[0].num, gathered[-1].num + 1))
                    if scattered:
                        pool.dma_reset(range(scattered[0].num, scattered[-1].num + 1))
                    for signal in (*in_round, *in_dense, *scattered):
                        pool.sem_clear(signal)

        GATHER_ROUNDS = ROUNDS - FIRST_ROUND
        FIRST = FIRST_ROUND * RING

        def dense_sum():
            BLOCKS = DENSE_GROUPS * TILES
            with nc.Block() as block:
                @block.gpsimd
                def _(pool):
                    with pool.Fori(0, GATHER_ROUNDS) as i:
                        for r in range(RING):
                            gather(pool, i, r)

                @block.sync
                def _(sp):
                    for g in range(DENSE_GROUPS):
                        with sp.Fori(g * TILES, (g + 1) * TILES) as u:
                            load_block(sp, u, dense_pieces[g][bass.ds(u - g * TILES, 1), :, :, :]
                                       .rearrange("t b p f -> (t b) p f"))

                @block.scalar
                def _(act):
                    for r in range(RING):
                        stage_edges(act, 0, r, FIRST)
                    with act.Fori(0, GATHER_ROUNDS - 1) as i:
                        for r in range(RING):
                            stage_next(act, i, r, FIRST)

                @block.tensor
                def _(pe):
                    slots_start_free(nc.tensor)
                    with pe.Fori(0, BLOCKS) as i:
                        multiply_both(pe, i, i)
                    with pe.Fori(BLOCKS, GATHER_ROUNDS) as i:
                        for r in range(RING):
                            multiply(pe, i, r)

                @block.vector
                def _(dve):
                    slots_start_free(nc.vector)
                    for g in range(DENSE_GROUPS):
                        with dve.Fori(g * TILES, (g + 1) * TILES) as i:
                            add_both(dve, i, i, i * WIDE + (START[g] - g * TILES * WIDE))
                    with dve.Fori(BLOCKS, GATHER_ROUNDS) as i:
                        add_windows(dve, i)
            clear_dense()

        STAGE_M = 4
        STAGES = 2
        place_now = sb("place_now", [P, STAGES, STAGE_M, CHUNKS], int32)
        place_w_now = sb("place_w_now", [P, STAGES, STAGE_M, CHUNKS])
        scattered = [sem(f"scattered{q}") for q in range(CHUNKS)]
        zero_set, zero_stored = sem("zero_set"), [sem(f"zero_stored{a}") for a in range(FILLS)]
        place_staged = sem("place_staged")
        in_build = [zero_set, *zero_stored, place_staged]
        STEPS = P // STAGE_M
        all_places = place[:, :, :, :].rearrange("p g m q -> p (g m q)")
        all_place_w = place_w[:, :, :, :].rearrange("p g m q -> p (g m q)")

        def scatter_step(pool, i2, k, g, first=False):
            pool.wait_ge(place_staged, i2 * (2 * 2) + (2 * k + 2))
            for m in range(STAGE_M):
                for q0 in (0, CHUNKS // 2):
                    if not (first and k == 0 and m == 0):
                        for q in range(q0, q0 + CHUNKS // 2):
                            pool.wait_ge(scattered[q], i2 * (32 * STAGE_M) + 16 * (STAGE_M * k + m))
                    pool.sem_inc(begun, 1)
                    for q in range(q0, q0 + CHUNKS // 2):
                        pool.indirect_dma_start(
                            dense[g][:, :], bass.IndirectOffsetOnAxis(ap=place_now[:, k, m, q:q + 1], axis=0),
                            place_w_now[:, k, m, q:q + 1], None, compute_op=ALU.add,
                        ).then_inc(scattered[q], 16)

        def stage_places(dve, i2, k, first=False):
            if not first:
                for q in range(CHUNKS):
                    dve.wait_ge(scattered[q], i2 * (32 * STAGE_M) + 16 * STAGE_M * (k - 1))
            width = STAGE_M * CHUNKS
            now = bass.ds(i2 * (2 * width) + k * width, width)
            dve.tensor_scalar(place_now[:, k, :, :].rearrange("p m q -> p (m q)"), all_places[:, now], 0,
                              None, ALU.bitwise_or).then_inc(place_staged, 1)
            dve.tensor_copy(place_w_now[:, k, :, :].rearrange("p m q -> p (m q)"), all_place_w[:, now])\
                .then_inc(place_staged, 1)

        def building_sum():
            HALF_STEPS = STEPS // STAGES
            FILL = PIECES * PIECE // FILLS
            ALL_ZERO = [16 * (g + 1) * TILES for g in range(DENSE_GROUPS)]
            BESIDE = TILES
            AFTER = DENSE_GROUPS * TILES - BESIDE
            BEFORE = GATHER_ROUNDS - AFTER
            assert HALF_STEPS <= TILES and BEFORE > 0 and DENSE_GROUPS == 2
            with nc.Block() as block:
                @block.gpsimd
                def _(pool):
                    with pool.Fori(0, BEFORE) as i:
                        for r in range(RING):
                            gather(pool, i, r)
                    for stored in zero_stored:
                        pool.wait_ge(stored, ALL_ZERO[0])
                    scatter_step(pool, 0, 0, 0, first=True)
                    scatter_step(pool, 0, 1, 0, first=True)
                    with pool.Fori(1, HALF_STEPS) as i2:
                        for k in range(STAGES):
                            scatter_step(pool, i2, k, 0)
                    for stored in zero_stored:
                        pool.wait_ge(stored, ALL_ZERO[1])
                    with pool.Fori(HALF_STEPS, 2 * HALF_STEPS) as i2:
                        for k in range(STAGES):
                            scatter_step(pool, i2, k, 1)
                    with pool.Fori(BEFORE, GATHER_ROUNDS) as i:
                        for r in range(RING):
                            gather(pool, i, r)

                @block.sync
                def _(sp):
                    sp.wait_ge(zero_set, 1)

                    def fill(u, target, first=False):
                        for a in range(FILLS):
                            if a >= 2:
                                sp.wait_ge(zero_stored[a - 2], u * 16 + 16)
                            elif not first:
                                sp.wait_ge(zero_stored[a - 2], u * 16)
                            sp.dma_start(target[a, :, :], arena[0:Q, 0:FILL]).then_inc(zero_stored[a], 16)

                    fill(0, dense_fills[0][0, :, :, :], first=True)
                    for g in range(DENSE_GROUPS):
                        with sp.Fori(max(1, g * TILES), (g + 1) * TILES) as u:
                            fill(u, dense_fills[g][bass.ds(u - g * TILES, 1), :, :, :]
                                 .rearrange("t a p f -> (t a) p f"))
                    for stored in zero_stored:
                        sp.wait_ge(stored, ALL_ZERO[-1])
                    for g in range(DENSE_GROUPS):
                        for q in range(CHUNKS):
                            sp.wait_ge(scattered[q], 16 * P * (g + 1))
                        with sp.Fori(g * TILES, (g + 1) * TILES) as u:
                            load_block(sp, u, dense_pieces[g][bass.ds(u - g * TILES, 1), :, :, :]
                                       .rearrange("t b p f -> (t b) p f"))

                @block.scalar
                def _(act):
                    for r in range(RING):
                        stage_edges(act, 0, r, FIRST)
                    with act.Fori(0, GATHER_ROUNDS - 1) as i:
                        for r in range(RING):
                            stage_next(act, i, r, FIRST)

                @block.tensor
                def _(pe):
                    slots_start_free(nc.tensor)
                    with pe.Fori(0, BEFORE) as i:
                        for r in range(RING):
                            multiply(pe, i, r)
                    with pe.Fori(0, BESIDE) as u:
                        multiply_block(pe, u, 0, PIECES)
                    with pe.Fori(BEFORE, GATHER_ROUNDS) as i:
                        multiply_both(pe, i, i - (BEFORE - BESIDE))

                @block.vector
                def _(dve):
                    dve.memset(arena[0:Q, 0:FILL], 0.0).then_inc(zero_set, 1)
                    slots_start_free(nc.vector)
                    with dve.Fori(0, BEFORE) as i:
                        add_windows(dve, i)
                    stage_places(dve, 0, 0, first=True)
                    stage_places(dve, 0, 1, first=True)
                    with dve.Fori(1, HALF_STEPS) as i2:
                        for k in range(STAGES):
                            stage_places(dve, i2, k)
                    with dve.Fori(0, HALF_STEPS) as u:
                        for k in range(STAGES):
                            stage_places(dve, u + HALF_STEPS, k)
                        add_block(dve, u, u * WIDE + START[0], before=(added, BEFORE * RING + RING))
                    with dve.Fori(HALF_STEPS, BESIDE) as u:
                        add_block(dve, u, u * WIDE + START[0])
                    late = BEFORE - BESIDE
                    with dve.Fori(BEFORE, GATHER_ROUNDS) as i:
                        add_both(dve, i, i - late, i * WIDE + (START[1] - (TILES + late) * WIDE))
            clear_dense(scattered)
            with nc.Block() as block:
                @block.gpsimd
                def _(pool):
                    for signal in in_build:
                        pool.sem_clear(signal)

        def weighted_sum(part):
            with nc.If(use_dense):
                part()
            with nc.Else():
                edge_sum()

        prepare()
        widest = nc.values_load(span_max[0:1, 0:1], min_val=0, max_val=N - 1)
        use_dense = nc.values_load(sorted_enough[0:1, 0:1], min_val=0, max_val=1)
        update("first", first=True)
        weighted_sum(building_sum)
        update("project")
        weighted_sum(dense_sum)
        update("add")
        weighted_sum(dense_sum)
        update("hop")
        weighted_sum(dense_sum)
        update("add")
        edge_sum(with_features=True)
        update("last")


def kernel(x, src, dst, edge_attr_48, edge_weight, L0_gnn_w, L0_gnn_b, L3_gnn_eps):
    import numpy as np
    import concourse.bacc as bacc
    from concourse import mybir
    from concourse.bass_utils import run_bass_kernel_spmd

    nc = bacc.Bacc("TRN2", target_bir_lowering=False, num_devices=1)
    given = {"x": x, "src": src, "dst": dst, "edge_attr": edge_attr_48, "edge_weight": edge_weight,
             "weight": L0_gnn_w, "bias": L0_gnn_b, "eps": L3_gnn_eps}
    arrays = {name: np.ascontiguousarray(a) for name, a in given.items()}
    aps = [nc.dram_tensor(name, a.shape, mybir.dt.from_np(a.dtype), kind="ExternalInput").ap()
           for name, a in arrays.items()]
    out = nc.dram_tensor("out", x.shape, mybir.dt.float32, kind="ExternalOutput").ap()
    gnn_kernel(nc, *aps, out)
    result = run_bass_kernel_spmd(nc, [arrays], core_ids=[0])
    return result.results[0]["out"]
```
